# Optimizing a Trainium2 kernel written in Bass

```python
import numpy as np
import jax
import jax.numpy as jnp

def _softmax(x, axis=-1):
    return jax.nn.softmax(x, axis=axis)

def _gelu(x):
    return jax.nn.gelu(x, approximate=True)

def _silu(x):
    return jax.nn.silu(x)

def _sigmoid(x):
    return jax.nn.sigmoid(x)

def _layernorm(x, axis=-1, eps=1e-05):
    m = jnp.mean(x, axis=axis, keepdims=True)
    v = jnp.var(x, axis=axis, keepdims=True)
    return (x - m) / jnp.sqrt(v + eps)

def _scatter_add(tgt, idx, src, axis=0):
    return tgt.at[idx].add(src)

def _segment_sum(src, seg, n):
    return jax.ops.segment_sum(src, seg, n)
kernel_name = 'mk_gps_d1_gnn_r32_f3b2b7'

def setup_inputs(seed: int=0):
    np.random.seed(seed)
    _w = jnp.asarray

    def _rec_inputs():
        import jax
        import jax.numpy as jnp
        _gk = jax.random.key(seed)
        x = -0.0003713 + 1 * jax.random.normal(jax.random.fold_in(_gk, 1), (3125, 256), jnp.float32)
        src = jax.random.randint(jax.random.fold_in(_gk, 2), (50000,), 0, 3125, jnp.int32)
        dst = jnp.minimum((3125 * jax.random.uniform(jax.random.fold_in(_gk, 3), (50000,)) ** 2.0).astype(jnp.int32), 99999)
        _o = jnp.argsort(dst, stable=True)
        src = src[_o]
        dst = dst[_o]
        edge_attr_64 = -9.77346e-05 + 0.999888 * jax.random.normal(jax.random.fold_in(_gk, 12), (50000, 64), jnp.float32)
        return (x, src, dst, edge_attr_64)
    x, src, dst, edge_attr_64 = _rec_inputs()

    def _L0_gnn_setup():
        import jax, jax.numpy as jnp
        import numpy as np
        N_NODES = 50000
        N_EDGES = 25000
        IN_DIM = 256
        E_DIM = 64
        N_HEADS = 8
        OUT_DIM = 32
        NEG_SLOPE = 0.2
        key = jax.random.key(seed)
        ks = jax.random.split(key, 10)
        return {'feat': jax.random.normal(ks[0], (N_NODES, IN_DIM), dtype=jnp.float32), 'edge_attr': jax.random.normal(ks[1], (N_EDGES, E_DIM), dtype=jnp.float32), 'src': jax.random.randint(ks[2], (N_EDGES,), 0, N_NODES, dtype=jnp.int32), 'dst': jax.random.randint(ks[3], (N_EDGES,), 0, N_NODES, dtype=jnp.int32), 'W_fc': jax.random.normal(ks[4], (IN_DIM, N_HEADS * OUT_DIM), dtype=jnp.float32) * (1.0 / np.sqrt(IN_DIM)), 'W_e': jax.random.normal(ks[5], (E_DIM, N_HEADS * OUT_DIM), dtype=jnp.float32) * (1.0 / np.sqrt(E_DIM)), 'attn_h': jax.random.normal(ks[6], (N_HEADS, OUT_DIM), dtype=jnp.float32) * 0.1, 'attn_e': jax.random.normal(ks[7], (N_HEADS, OUT_DIM), dtype=jnp.float32) * 0.1, 'attn_t': jax.random.normal(ks[8], (N_HEADS, OUT_DIM), dtype=jnp.float32) * 0.1, 'bias': jnp.zeros((N_HEADS, OUT_DIM), dtype=jnp.float32)}
    _L0_gnn_all = _L0_gnn_setup()
    _L0_gnn_in = {k: v for k, v in _L0_gnn_all.items() if k in ('W_fc', 'W_e', 'attn_h', 'attn_e', 'attn_t', 'bias')}
    del _L0_gnn_all

    def _L0_mix_setup():
        import jax, jax.numpy as jnp
        import numpy as np
        A, Bc, Cc = (0.5, 1.0, 1.0)
        H = 8
        EPS = 1e-12

        def _normalize(t):
            n = jnp.linalg.norm(t, axis=-1, keepdims=True)
            return t / jnp.maximum(n, EPS)
        key = jax.random.key(seed)
        ks = jax.random.split(key, 5)
        B, N, C = (8, 64, 256)
        D = C // H
        x = jax.random.normal(ks[0], (B, N, C), dtype=jnp.float32)
        Wqkv = jax.random.normal(ks[1], (3 * H * D, C), dtype=jnp.float32) * 0.02
        bqkv = jnp.zeros((3 * H * D,), dtype=jnp.float32)
        Wproj = jax.random.normal(ks[2], (C, H * D), dtype=jnp.float32) * 0.02
        bproj = jnp.zeros((C,), dtype=jnp.float32)
        temperature = jnp.ones((1, H, 1, 1), dtype=jnp.float32)
        return {'x': x, 'Wqkv': Wqkv, 'bqkv': bqkv, 'Wproj': Wproj, 'bproj': bproj, 'temperature': temperature}
    _L0_mix_all = _L0_mix_setup()
    _L0_mix_in = {k: v for k, v in _L0_mix_all.items() if k in ('Wqkv', 'bqkv', 'Wproj', 'bproj', 'temperature')}
    del _L0_mix_all

    def _L0_ffn_setup():
        import jax, jax.numpy as jnp
        import numpy as np
        B, N, D = (16, 128, 256)
        NUM_EXPERTS, TOP_K, HEADS = (4, 2, 4)
        N_EDGES = 32768
        LN_EPS = 1e-05

        def _layernorm(x, g, b):
            mu = x.mean(-1, keepdims=True)
            var = ((x - mu) ** 2).mean(-1, keepdims=True)
            return (x - mu) * jax.lax.rsqrt(var + LN_EPS) * g + b

        def _forward(x, edge_index, W_gat, att_src, att_dst, b_gat, ln_gamma, ln_beta, W1, b1, W2, b2):
            Bc, Nc, Dc = x.shape
            M = Bc * Nc
            x_flat = x.reshape(M, Dc)
            h = (x_flat @ W_gat).reshape(M, HEADS, NUM_EXPERTS)
            loops = jnp.arange(M, dtype=edge_index.dtype)
            src = jnp.concatenate([edge_index[0], loops])
            dst = jnp.concatenate([edge_index[1], loops])
            a_src = (h * att_src).sum(-1)
            a_dst = (h * att_dst).sum(-1)
            e = jax.nn.leaky_relu(a_src[src] + a_dst[dst], negative_slope=0.2)
            e_max = jax.ops.segment_max(e, dst, num_segments=M)
            ee = jnp.exp(e - e_max[dst])
            denom = jax.ops.segment_sum(ee, dst, num_segments=M)
            alpha = ee / (denom[dst] + 1e-16)
            msg = h[src] * alpha[:, :, None]
            agg = jax.ops.segment_sum(msg, dst, num_segments=M).reshape(M, HEADS * NUM_EXPERTS) + b_gat
            scores = _layernorm(agg, ln_gamma, ln_beta).reshape(M, HEADS, NUM_EXPERTS).mean(1)
            scores = scores.reshape(Bc, Nc, NUM_EXPERTS)
            topk_s, topk_i = jax.lax.top_k(scores, TOP_K)
            w = jax.nn.softmax(topk_s, axis=-1)
            out = jnp.zeros_like(x)
            for ei in range(NUM_EXPERTS):
                g = jnp.where(topk_i == ei, w, 0.0).sum(-1)
                hh = jax.nn.gelu(x @ W1[ei] + b1[ei], approximate=False)
                out = out + g[..., None] * (hh @ W2[ei] + b2[ei])
            return out
        key = jax.random.key(seed)
        ks = jax.random.split(key, 8)
        s = 0.05
        return {'x': jax.random.normal(ks[0], (B, N, D), jnp.float32), 'W_gat': jax.random.normal(ks[1], (D, HEADS * NUM_EXPERTS), jnp.float32) * s, 'att_src': jax.random.normal(ks[2], (HEADS, NUM_EXPERTS), jnp.float32) * s, 'att_dst': jax.random.normal(ks[3], (HEADS, NUM_EXPERTS), jnp.float32) * s, 'b_gat': jnp.zeros((HEADS * NUM_EXPERTS,), jnp.float32), 'ln_gamma': jnp.ones((HEADS * NUM_EXPERTS,), jnp.float32), 'ln_beta': jnp.zeros((HEADS * NUM_EXPERTS,), jnp.float32), 'W1': jax.random.normal(ks[4], (NUM_EXPERTS, D, 2 * D), jnp.float32) * s, 'b1': jnp.zeros((NUM_EXPERTS, 2 * D), jnp.float32), 'W2': jax.random.normal(ks[5], (NUM_EXPERTS, 2 * D, D), jnp.float32) * s, 'b2': jnp.zeros((NUM_EXPERTS, D), jnp.float32), 'edge_index': jax.random.randint(ks[6], (2, N_EDGES), 0, B * N, jnp.int32)}
    _L0_ffn_all = _L0_ffn_setup()
    _L0_ffn_in = {k: v for k, v in _L0_ffn_all.items() if k in ('W_gat', 'att_src', 'att_dst', 'b_gat', 'ln_gamma', 'ln_beta', 'W1', 'b1', 'W2', 'b2', 'edge_index')}
    del _L0_ffn_all
    return {'x': x, 'src': src, 'dst': dst, 'edge_attr_64': edge_attr_64, 'L0_gnn_W_fc': _L0_gnn_in['W_fc'], 'L0_gnn_W_e': _L0_gnn_in['W_e'], 'L0_gnn_attn_h': _L0_gnn_in['attn_h'], 'L0_gnn_attn_e': _L0_gnn_in['attn_e'], 'L0_gnn_attn_t': _L0_gnn_in['attn_t'], 'L0_gnn_bias': _L0_gnn_in['bias'], 'L0_mix_Wqkv': _L0_mix_in['Wqkv'], 'L0_mix_bqkv': _L0_mix_in['bqkv'], 'L0_mix_Wproj': _L0_mix_in['Wproj'], 'L0_mix_bproj': _L0_mix_in['bproj'], 'L0_mix_temperature': _L0_mix_in['temperature'], 'L0_ffn_W_gat': _L0_ffn_in['W_gat'], 'L0_ffn_att_src': _L0_ffn_in['att_src'], 'L0_ffn_att_dst': _L0_ffn_in['att_dst'], 'L0_ffn_b_gat': _L0_ffn_in['b_gat'], 'L0_ffn_ln_gamma': _L0_ffn_in['ln_gamma'], 'L0_ffn_ln_beta': _L0_ffn_in['ln_beta'], 'L0_ffn_W1': _L0_ffn_in['W1'], 'L0_ffn_b1': _L0_ffn_in['b1'], 'L0_ffn_W2': _L0_ffn_in['W2'], 'L0_ffn_b2': _L0_ffn_in['b2'], 'L0_ffn_edge_index': _L0_ffn_in['edge_index']}

def reference(x, src, dst, edge_attr_64, L0_gnn_W_fc, L0_gnn_W_e, L0_gnn_attn_h, L0_gnn_attn_e, L0_gnn_attn_t, L0_gnn_bias, L0_mix_Wqkv, L0_mix_bqkv, L0_mix_Wproj, L0_mix_bproj, L0_mix_temperature, L0_ffn_W_gat, L0_ffn_att_src, L0_ffn_att_dst, L0_ffn_b_gat, L0_ffn_ln_gamma, L0_ffn_ln_beta, L0_ffn_W1, L0_ffn_b1, L0_ffn_W2, L0_ffn_b2, L0_ffn_edge_index):
    import jax
    import jax.numpy as jnp

    def _L0_gnn_ref(feat, edge_attr, src, dst, W_fc, W_e, attn_h, attn_e, attn_t, bias):
        import jax, jax.numpy as jnp
        import numpy as np
        N_NODES = 50000
        N_EDGES = 25000
        IN_DIM = 256
        E_DIM = 64
        N_HEADS = 8
        OUT_DIM = 32
        NEG_SLOPE = 0.2
        N = feat.shape[0]
        H, D = attn_h.shape
        ft = (feat @ W_fc).reshape(N, H, D)
        eh = jnp.einsum('nhd,hd->nh', ft, attn_h)
        et = jnp.einsum('nhd,hd->nh', ft, attn_t)
        fe = (edge_attr @ W_e).reshape(-1, H, D)
        ee = jnp.einsum('ehd,hd->eh', fe, attn_e)
        e = jax.nn.leaky_relu(eh[src] + ee + et[dst], negative_slope=NEG_SLOPE)
        e_max = jax.ops.segment_max(e, dst, num_segments=N)
        e_max = jax.lax.stop_gradient(jnp.where(jnp.isfinite(e_max), e_max, 0.0))
        ex = jnp.exp(e - e_max[dst])
        denom = jax.ops.segment_sum(ex, dst, num_segments=N)
        a = ex / denom[dst]
        msg = ft[src] * a[:, :, None]
        rst = jax.ops.segment_sum(msg, dst, num_segments=N)
        rst = rst + bias[None, :, :]
        return rst.reshape(N, H * D)

    def _L0_mix_ref(x, Wqkv, bqkv, Wproj, bproj, temperature):
        import jax, jax.numpy as jnp
        import numpy as np
        A, Bc, Cc = (0.5, 1.0, 1.0)
        H = 8
        EPS = 1e-12

        def _normalize(t):
            n = jnp.linalg.norm(t, axis=-1, keepdims=True)
            return t / jnp.maximum(n, EPS)
        B, N, C = x.shape
        D = C // H
        scale = float(D) ** 0.25
        qkv = (x @ Wqkv.T + bqkv).reshape(B, N, 3, H, D)
        qkv = jnp.transpose(qkv, (2, 0, 3, 1, 4))
        q, k, v = (qkv[0], qkv[1], qkv[2])
        q = q * scale
        v1 = jnp.concatenate([jnp.ones((B, H, N, 1), dtype=v.dtype), v], axis=-1)
        qn = _normalize(q) * (scale * temperature)
        kn = _normalize(k) * scale
        vN = v1 / N
        kv_mod = jnp.einsum('bhni,bhnj,bhne->bhije', kn, kn, vN)
        kv = jnp.einsum('bhnd,bhne->bhde', kn, vN)
        vsum = jnp.sum(vN, axis=-2)[:, :, None, :]
        y = A * jnp.einsum('bhni,bhnj,bhije->bhne', qn, qn, kv_mod) + scale ** 2 * Bc * jnp.einsum('bhnd,bhde->bhne', qn, kv) + scale ** 4 * Cc * vsum
        y_norm, y = (y[..., :1], y[..., 1:])
        y = y / y_norm
        out = jnp.transpose(y, (0, 2, 1, 3)).reshape(B, N, H * D)
        return out @ Wproj.T + bproj

    def _L0_ffn_ref(x, W_gat, att_src, att_dst, b_gat, ln_gamma, ln_beta, W1, b1, W2, b2, edge_index):
        import jax, jax.numpy as jnp
        import numpy as np
        B, N, D = (16, 128, 256)
        NUM_EXPERTS, TOP_K, HEADS = (4, 2, 4)
        N_EDGES = 32768
        LN_EPS = 1e-05

        def _layernorm(x, g, b):
            mu = x.mean(-1, keepdims=True)
            var = ((x - mu) ** 2).mean(-1, keepdims=True)
            return (x - mu) * jax.lax.rsqrt(var + LN_EPS) * g + b

        def _forward(x, edge_index, W_gat, att_src, att_dst, b_gat, ln_gamma, ln_beta, W1, b1, W2, b2):
            Bc, Nc, Dc = x.shape
            M = Bc * Nc
            x_flat = x.reshape(M, Dc)
            h = (x_flat @ W_gat).reshape(M, HEADS, NUM_EXPERTS)
            loops = jnp.arange(M, dtype=edge_index.dtype)
            src = jnp.concatenate([edge_index[0], loops])
            dst = jnp.concatenate([edge_index[1], loops])
            a_src = (h * att_src).sum(-1)
            a_dst = (h * att_dst).sum(-1)
            e = jax.nn.leaky_relu(a_src[src] + a_dst[dst], negative_slope=0.2)
            e_max = jax.ops.segment_max(e, dst, num_segments=M)
            ee = jnp.exp(e - e_max[dst])
            denom = jax.ops.segment_sum(ee, dst, num_segments=M)
            alpha = ee / (denom[dst] + 1e-16)
            msg = h[src] * alpha[:, :, None]
            agg = jax.ops.segment_sum(msg, dst, num_segments=M).reshape(M, HEADS * NUM_EXPERTS) + b_gat
            scores = _layernorm(agg, ln_gamma, ln_beta).reshape(M, HEADS, NUM_EXPERTS).mean(1)
            scores = scores.reshape(Bc, Nc, NUM_EXPERTS)
            topk_s, topk_i = jax.lax.top_k(scores, TOP_K)
            w = jax.nn.softmax(topk_s, axis=-1)
            out = jnp.zeros_like(x)
            for ei in range(NUM_EXPERTS):
                g = jnp.where(topk_i == ei, w, 0.0).sum(-1)
                hh = jax.nn.gelu(x @ W1[ei] + b1[ei], approximate=False)
                out = out + g[..., None] * (hh @ W2[ei] + b2[ei])
            return out
        return _forward(x, edge_index, W_gat, att_src, att_dst, b_gat, ln_gamma, ln_beta, W1, b1, W2, b2)
    xn = _layernorm(x, axis=-1)
    x = x + _L0_gnn_ref(xn, edge_attr_64, src, dst, L0_gnn_W_fc, L0_gnn_W_e, L0_gnn_attn_h, L0_gnn_attn_e, L0_gnn_attn_t, L0_gnn_bias) + _L0_mix_ref(xn[None], L0_mix_Wqkv, L0_mix_bqkv, L0_mix_Wproj, L0_mix_bproj, L0_mix_temperature)[0]
    x = x + _L0_ffn_ref(_layernorm(x, axis=-1)[None], L0_ffn_W_gat, L0_ffn_att_src, L0_ffn_att_dst, L0_ffn_b_gat, L0_ffn_ln_gamma, L0_ffn_ln_beta, L0_ffn_W1, L0_ffn_b1, L0_ffn_W2, L0_ffn_b2, L0_ffn_edge_index)[0]
    return x

_drawn_inputs = setup_inputs


def setup_inputs(seed=0):
    import zlib

    import numpy as np

    out = dict(_drawn_inputs(seed))
    spreads = {'L0_gnn_bias': (0.0, 0.1),
     'L0_mix_bqkv': (0.0, 0.1),
     'L0_mix_bproj': (0.0, 0.1),
     'L0_mix_temperature': (1.0, 0.6),
     'L0_ffn_b_gat': (0.0, 0.1),
     'L0_ffn_ln_gamma': (1.0, 0.2),
     'L0_ffn_ln_beta': (0.0, 0.1),
     'L0_ffn_b1': (0.0, 0.1),
     'L0_ffn_b2': (0.0, 0.1)}
    factors = {'L0_mix_Wqkv': 4.476}
    for name, (base, spread) in spreads.items():
        noise = np.random.default_rng([zlib.crc32(name.encode()), seed]).standard_normal(out[name].shape)
        drawn = base * np.exp(spread * noise) if base else spread * noise
        out[name] = jnp.asarray(drawn.astype(out[name].dtype))
    for name, factor in factors.items():
        out[name] = (out[name] * factor).astype(out[name].dtype)
    return out
```

```python
from contextlib import ExitStack

import concourse.bass as bass
from concourse import mybir

F32 = mybir.dt.float32
BF16 = mybir.dt.bfloat16
I32 = mybir.dt.int32
ALU = mybir.AluOpType
ACT = mybir.ActivationFunctionType
AX_X = mybir.AxisListType.X
RMAX = bass.bass_isa.ReduceOp.max

P = 128
N = 3125
T = (N + P - 1) // P
NT = T * P
C = 256
CB = C // P
H, D = 8, 32
HALF = H // CB
E = 50000
K4 = 4
GE = K4 * P
G1 = (E + GE - 1) // GE
ED = 64
PAIRS = 8
WN = P
NW = NT + WN
TF = C + H
FF = C + 2 * H
MSG = C + 32
TAIL = 16 + D + 1
DUP = D + 16
SC = float(D) ** 0.25
E2 = 32768
G2 = E2 // GE
H2, X = 4, 4
HC = H2 * X
R2 = HC + H2
HID = 512
HB = HID // P
EPS_LN = 1e-5
EPS_N = 1e-12
FAR = 8192.0
TINY = 1e-37


def wait(eng, sem, value):
    eng.wait_ge(sem, value)
    if not isinstance(value, int):
        eng.nop(nofuse=True)


class Chain:

    def __init__(self, eng, sem):
        self.eng, self.sem, self.base, self.n = eng, sem, 0, 0

    def __call__(self, ins):
        ins.then_inc(self.sem, 1)
        self.n += 1
        wait(self.eng, self.sem, self.base + self.n)

    def enter(self, i, per):
        self.start, self.per = self.base + self.n, per
        self.base, self.n = self.start + i * per, 0

    def leave(self, turns):
        assert self.n == self.per, (self.n, self.per)
        self.base, self.n = self.start + turns * self.per, 0


def prepare(nc, io, keep, dram):
    with ExitStack() as ctx:
        def sb(name, shape, dt=F32):
            return ctx.enter_context(nc.sbuf_tensor(name, shape, dt))

        def psum(name):
            return ctx.enter_context(nc.psum_tensor(name, [P, 512], F32))

        def sem(name):
            return ctx.enter_context(nc.semaphore(name))

        wf = sb("wf", [P, CB, FF])
        ah, at, ae = sb("ah", [P, C]), sb("at", [P, C]), sb("ae", [P, C])
        we = sb("we", [P, C])
        prod = sb("prod", [P, CB, C])
        wee = sb("wee", [P, H])
        wbd = sb("wbd", [P, 2 * H])
        ea = [sb(f"ea{b}", [P, PAIRS * P]) for b in range(2)]
        stats, agg = sb("stats", [P, 6]), sb("agg", [P, 2])
        mv = sb("mv", [P, T, 2])
        vare, rstd, half = sb("vare", [P, T]), sb("rstd", [P, T]), sb("half", [P, T])
        xn = [sb(f"xn{b}", [P, C]) for b in range(2)]
        xt = [sb(f"xt{b}", [P, CB, P]) for b in range(2)]
        frow = [sb(f"frow{b}", [P, FF]) for b in range(2)]
        ehet = sb("ehet", [P, T, 2 * H])
        dsti, dstf, dstb = sb("dsti", [P, G1 + 1, K4], I32), sb("dstf", [P, G1 + 1, K4]), sb("dstb", [P, G1 + 1, K4])
        nred = 4 * H + 2 * (G1 + 1)
        red, redall = sb("red", [P, nred]), sb("redall", [P, nred])
        basef = sb("basef", [P, G1 + 1])
        etp = sb("etp", [P, T, 3 * H], BF16)
        etr = sb("etr", [P, T, H])
        ztail = sb("ztail", [P, 3 * H], BF16)
        psX = [psum(f"psX{b}") for b in range(2)]
        psF = [psum(f"psF{b}") for b in range(2)]
        psEE = [psum(f"psEE{b}") for b in range(2)]

        loaded, x_loaded = sem("loaded"), sem("x_loaded")
        ea_loaded = [sem(f"ea_loaded{b}") for b in range(2)]
        v_step, p_step = sem("v_step"), sem("p_step")
        weights_made, var_made, rstd_made = sem("weights_made"), sem("var_made"), sem("rstd_made")
        ident_made = sem("ident_made")
        xn_made, xn_turned, xt_copied = sem("xn_made"), sem("xn_turned"), sem("xt_copied")
        ee_summed, f_summed = sem("ee_summed"), sem("f_summed")
        f_copied, ee_copied = sem("f_copied"), sem("ee_copied")
        row_stored = [sem(f"row_stored{b}") for b in range(2)]
        red_made, red_all = sem("red_made"), sem("red_all")
        et_made, et_stored = sem("et_made"), sem("et_stored")
        block = ctx.enter_context(nc.Block())
        LOADS = 7

        @block.sync
        def _(sp):
            sp.dma_start(keep.x[:], io["x"].rearrange("(t p) c -> p t c", p=P)).then_inc(x_loaded, 16)
            sp.dma_start(wf[:, :, 0:C], io["W_fc"].rearrange("(c p) n -> p c n", p=P)).then_inc(loaded, 16)
            sp.dma_start(ah[:], io["attn_h"].broadcast_to([P, C])).then_inc(loaded, 16)
            sp.dma_start(at[:], io["attn_t"].broadcast_to([P, C])).then_inc(loaded, 16)
            sp.dma_start(ae[:], io["attn_e"].broadcast_to([P, C])).then_inc(loaded, 16)
            sp.dma_start(we[0:ED, :], io["W_e"]).then_inc(loaded, 16)
            sp.dma_start(we[ED:P, :], io["W_e"]).then_inc(loaded, 16)
            sp.dma_start(dsti[:], io["dst"]).then_inc(loaded, 16)

            def load_edges(t, b, before):
                if before is not None:
                    wait(sp, ee_summed, before)
                sp.dma_start(ea[b][:], io["edge"][:, bass.ds(t * PAIRS * P, PAIRS * P)]).then_inc(ea_loaded[b], 16)

            def store_row(t, b):
                wait(sp, f_copied, t + 1)
                sp.dma_start(dram.table[bass.ds(t * P, P), :], frow[b][:, 0:TF]).then_inc(row_stored[b], 16)

            load_edges(0, 0, None)
            load_edges(1, 1, None)
            with sp.Fori(0, T // 2) as i:
                for b in range(2):
                    store_row(i * 2 + b, b)
                    load_edges(i * 2 + b + 2, b, i * 2 + b + 1)
            store_row(T - 1, 0)
            sp.wait_ge(et_made, 3)
            sp.dma_start(dram.et[0:NT, :].rearrange("(t p) c -> p t c", p=P), etp[:]).then_inc(et_stored, 16)
            sp.dma_start(dram.et[NT:NW, :], ztail[:]).then_inc(et_stored, 16)
            sp.wait_ge(et_stored, 32)
            sp.wait_ge(row_stored[0], 16 * (T // 2 + 1))
            sp.wait_ge(row_stored[1], 16 * (T // 2))
            sp.wait_ge(ea_loaded[0], 16 * (T // 2 + 1))
            sp.wait_ge(ea_loaded[1], 16 * (T // 2 + 1))

        @block.gpsimd
        def _(pool):
            step = Chain(pool, p_step)
            step(pool.memset(keep.ident[:], 0.0))
            pool.affine_select(out=keep.ident[:], in_=keep.ident[:], compare_op=ALU.not_equal, fill=1.0, base=0,
                               pattern=[[-1, P]], channel_multiplier=1).then_inc(ident_made, 1)
            pool.wait_ge(ident_made, 1)
            step(pool.iota(keep.iota[:], pattern=[[1, P]], base=0, channel_multiplier=0,
                           allow_small_or_imprecise_dtypes=True))
            step(pool.memset(keep.sel8[:], 0.0))
            for k in range(K4):
                step(pool.affine_select(out=keep.sel8[:], in_=keep.sel8[:], compare_op=ALU.not_equal, fill=1.0,
                                        base=-32 * k, pattern=[[-1, H]], channel_multiplier=1))
            step(pool.memset(keep.ones[:], 0.0))
            for h in range(HALF):
                step(pool.memset(keep.ones[D * h:D * h + D, D * h:D * h + D], 1.0))
            step(pool.memset(half[:], -0.5))
            pool.wait_ge(var_made, 1)
            pool.tensor_tensor(rstd[:], vare[:], half[:], ALU.pow).then_inc(rstd_made, 1)
            pool.wait_ge(red_made, 6)
            pool.partition_all_reduce(redall[:], red[:], P, RMAX).then_inc(red_all, 1)

        @block.vector
        def _(v):
            step = Chain(v, v_step)
            v.memset(keep.vrow[:, 0:N], 1.0)
            v.memset(keep.vrow[:, N:NT], 0.0)
            v.wait_ge(loaded, 16 * LOADS)
            for n, vec in enumerate((ah, at)):
                step(v.tensor_tensor(prod[:], wf[:, :, 0:C], vec[:].unsqueeze(1).broadcast_to([P, CB, C]), ALU.mult))
                step(v.tensor_reduce(wf[:, :, C + n * H:C + n * H + H],
                                     prod[:].rearrange("p c (h d) -> p c h d", h=H), AX_X, ALU.add))
            step(v.tensor_tensor(prod[:, 0, :], we[:], ae[:], ALU.mult))
            step(v.tensor_reduce(wee[:], prod[:, 0, :].rearrange("p (h d) -> p h d", h=H), AX_X, ALU.add))
            step(v.memset(wbd[:], 0.0))
            v.tensor_copy(wbd[0:ED, 0:H], wee[0:ED, :]).then_inc(weights_made, 1)
            v.tensor_copy(wbd[ED:P, H:2 * H], wee[ED:P, :]).then_inc(weights_made, 1)
            v.wait_ge(x_loaded, 16)
            with v.Fori(0, T) as t:
                step.enter(t, 3)
                step(v.bn_stats(stats[:], keep.x[:, bass.ds(t, 1), :].rearrange("p a c -> p (a c)")))
                step(v.bn_aggr(agg[:], stats[:]))
                step(v.tensor_copy(mv[:, bass.ds(t, 1), :].rearrange("p a c -> p (a c)"), agg[:]))
                step.leave(T)
            v.tensor_scalar(vare[:], mv[:, :, 1], EPS_LN, None, ALU.add).then_inc(var_made, 1)
            step(v.tensor_copy(dstf[:], dsti[:]))
            step(v.tensor_scalar(dstb[:], dstf[:], 0.0, FAR, ALU.is_lt, ALU.mult))
            step(v.tensor_tensor(dstb[:], dstb[:], dstf[:], ALU.add))
            step(v.tensor_scalar(dstb[:], dstb[:], -1.0, None, ALU.mult))
            v.tensor_reduce(red[:, 4 * H:4 * H + G1 + 1], dstb[:], AX_X, ALU.max).then_inc(red_made, 1)
            v.tensor_reduce(red[:, 4 * H + G1 + 1:nred], dstf[:], AX_X, ALU.max).then_inc(red_made, 1)
            v.wait_ge(rstd_made, 1)

            def norm(t, b, before):
                if before is not None:
                    wait(v, xn_turned, before)
                v.tensor_scalar(xn[b][:], keep.x[:, bass.ds(t, 1), :].rearrange("p a c -> p (a c)"),
                                mv[:, bass.ds(t, 1), 0:1].rearrange("p a c -> p (a c)"), rstd[:, bass.ds(t, 1)],
                                ALU.subtract, ALU.mult).then_inc(xn_made, 1)

            norm(0, 0, None)
            norm(1, 1, None)
            with v.Fori(0, T // 2 - 1) as i:
                for b in range(2):
                    norm(i * 2 + b + 2, b, i * 2 + b + 1)
            norm(T - 1, 0, T - 2)
            v.wait_ge(f_copied, T)
            for n, view in enumerate((ehet[:, :, 0:H].rearrange("p t h -> p h t"),
                                      keep.ee[:].rearrange("p (t h) -> p h t", h=H))):
                v.tensor_reduce(red[:, n * H:n * H + H], view, AX_X, ALU.max).then_inc(red_made, 1)
                step(v.tensor_reduce(red[:, (n + 2) * H:(n + 3) * H], view, AX_X, ALU.min))
                v.tensor_scalar(red[:, (n + 2) * H:(n + 3) * H], red[:, (n + 2) * H:(n + 3) * H], -1.0, None,
                                ALU.mult).then_inc(red_made, 1)
            step(v.memset(ztail[:], 0.0))
            et = ehet[:, :, H:2 * H]
            v.tensor_copy(etp[:, :, 0:H], et).then_inc(et_made, 1)
            v.wait_ge(et_made, 1)
            step(v.tensor_tensor(etr[:], et, etp[:, :, 0:H], ALU.subtract))
            v.tensor_copy(etp[:, :, H:2 * H], etr[:]).then_inc(et_made, 1)
            v.wait_ge(et_made, 2)
            v.tensor_tensor(etp[:, :, 2 * H:3 * H], etr[:], etp[:, :, H:2 * H], ALU.subtract).then_inc(et_made, 1)
            v.wait_ge(red_all, 1)
            step(v.tensor_tensor(keep.bound[:], redall[:, 0:H], redall[:, H:2 * H], ALU.add))
            step(v.tensor_scalar(basef[:], redall[:, 4 * H:4 * H + G1 + 1], -1.0, float(NT - 1), ALU.mult, ALU.min))
            step(v.tensor_copy(keep.base[:], basef[:]))
            step(v.tensor_tensor(keep.rel[:], dstf[:], basef[:].unsqueeze(2).broadcast_to([P, G1 + 1, K4]),
                                 ALU.subtract))

        @block.tensor
        def _(pe):
            pe.wait_ge(ident_made, 1)
            pe.wait_ge(weights_made, 2)

            def tile(t, b, later):
                wait(pe, xn_made, t + 1)
                if later is not None:
                    wait(pe, xt_copied, t - 1)
                for c in range(CB):
                    last = pe.transpose(psX[b][:, c * P:c * P + P], xn[b][:, c * P:c * P + P], keep.ident[:])
                last.then_inc(xn_turned, 1)
                wait(pe, ea_loaded[b], (t // 2) * 16 + 16 if isinstance(t, int) else later * 16 + 16)
                if later is not None:
                    wait(pe, ee_copied, t - 1)
                for j in range(PAIRS):
                    last = pe.matmul(psEE[b][:, j * 2 * H:(j + 1) * 2 * H], ea[b][:, j * P:j * P + P], wbd[:],
                                     start=True, stop=True)
                last.then_inc(ee_summed, 1)
                wait(pe, xt_copied, t + 1)
                if later is not None:
                    wait(pe, f_copied, t - 1)
                for c in range(CB):
                    last = pe.matmul(psF[b][:, 0:FF], xt[b][:, c, :], wf[:, c, :], start=(c == 0), stop=(c == CB - 1))
                last.then_inc(f_summed, 1)

            tile(0, 0, None)
            tile(1, 1, None)
            with pe.Fori(1, T // 2) as i:
                for b in range(2):
                    tile(i * 2 + b, b, i)
            tile(T - 1, 0, T // 2)

        @block.scalar
        def _(act):
            def tile(t, b, stored):
                wait(act, xn_turned, t + 1)
                xv = psX[b][:, 0:C].rearrange("p (c n) -> p c n", c=CB)
                act.copy(keep.xT[:, :, bass.ds(t * P, P)], xv)
                if stored is not None:
                    wait(act, f_summed, t - 1)
                act.copy(xt[b][:], xv).then_inc(xt_copied, 1)
                wait(act, ee_summed, t + 1)
                act.copy(keep.ee[:, bass.ds(t * PAIRS * 2 * H, PAIRS * 2 * H)],
                         psEE[b][:, 0:PAIRS * 2 * H]).then_inc(ee_copied, 1)
                wait(act, f_summed, t + 1)
                act.copy(ehet[:, bass.ds(t, 1), :].rearrange("p a h -> p (a h)"), psF[b][:, C:FF])
                if stored is not None:
                    wait(act, row_stored[b], stored)
                act.copy(frow[b][:], psF[b][:, 0:FF]).then_inc(f_copied, 1)

            tile(0, 0, None)
            tile(1, 1, None)
            with act.Fori(1, T // 2) as i:
                for b in range(2):
                    tile(i * 2 + b, b, i * 16)
            tile(T - 1, 0, (T // 2) * 16)


def attend(nc, io, keep, dram):
    with ExitStack() as ctx:
        def sb(name, shape, dt=F32):
            return ctx.enter_context(nc.sbuf_tensor(name, shape, dt))

        def psum(name):
            return ctx.enter_context(nc.psum_tensor(name, [P, 512], F32))

        def sem(name):
            return ctx.enter_context(nc.semaphore(name))

        idx = [sb(f"idx{b}", [P, K4], I32) for b in range(2)]
        etw = [sb(f"etw{b}", [P, 3 * H], BF16) for b in range(2)]
        got = [sb(f"got{b}", [P, K4, TF]) for b in range(2)]
        msg = [sb(f"msg{b}", [P, K4, MSG]) for b in range(2)]
        oh = [sb(f"oh{b}", [P, K4, WN]) for b in range(2)]
        ohT = [sb(f"ohT{b}", [P, K4, P], BF16) for b in range(2)]
        lg, lb = sb("lg", [P, K4, H]), sb("lb", [P, K4, H])
        wqkv = sb("wqkv", [P, CB, 3 * C])
        bqkv = sb("bqkv", [1, 3 * C])
        wproj = sb("wproj", [P, CB, C])
        temp = sb("temp", [P, H])
        xs = sb("xs", [P, CB, P])
        vs = sb("vs", [1, P])
        sq = sb("sq", [P, C])
        ss, rn, mhalf, rq = sb("ss", [P, H]), sb("rn", [P, H]), sb("mhalf", [P, H]), sb("rq", [P, H])
        vt = sb("vt", [P, C])
        dup = sb("dup", [P, H, DUP])
        phi = sb("phi", [P, H, 16, D])
        tail = sb("tail", [P, H, TAIL])
        far, unit = sb("far", [P, P]), sb("unit", [P, C])
        zero = sb("zero", [P, 512])
        kvt = sb("kvt", [P, 512])
        diag = sb("diag", [P, P])
        kv = sb("kv", [P, CB, 4, P])
        kv16 = sb("kv16", [P, CB, P])
        kvlin = sb("kvlin", [P, CB, P])
        gram = sb("gram", [P, CB, P])
        ksum, vsum = sb("ksum", [P, CB]), sb("vsum", [P, CB])
        phiT = sb("phiT", [P, 36, P])
        wq = sb("wq", [P, CB, P])
        rec = sb("rec", [P, CB, P])
        mixT = sb("mixT", [P, CB, P])
        psT, psE, psS, psP = psum("psT"), psum("psE"), psum("psS"), psum("psP")
        acc = [psum("psKA"), psum("psKB")]
        accT = psum("psKC")
        psU = psum("psU")

        loaded, filled, v_step, p_step = sem("loaded"), sem("filled"), sem("v_step"), sem("p_step")
        idx_loaded = [sem(f"idx_loaded{b}") for b in range(2)]
        etw_loaded = [sem(f"etw_loaded{b}") for b in range(2)]
        got_rows = [sem(f"got_rows{b}") for b in range(2)]
        oh_made, oh_turned, ohT_made, et_found = sem("oh_made"), sem("oh_turned"), sem("ohT_made"), sem("et_found")
        logits_made, exp_made, msg_made = sem("logits_made"), sem("exp_made"), sem("msg_made")
        scattered, added = sem("scattered"), sem("added")
        xs_made, projected, squared, ss_made, rn_made = (sem("xs_made"), sem("projected"), sem("squared"),
                                                         sem("ss_made"), sem("rn_made"))
        phi_made, k_summed, phi_turned, phiT_made = sem("phi_made"), sem("k_summed"), sem("phi_turned"), sem("phiT_made")
        kv_laid, kv_turned, kv_copied = sem("kv_laid"), sem("kv_turned"), sem("kv_copied")
        y_summed, wq_made, norm_summed, mix_made, out_summed, x_added = (
            sem("y_summed"), sem("wq_made"), sem("norm_summed"), sem("mix_made"), sem("out_summed"), sem("x_added"))
        block = ctx.enter_context(nc.Block())

        @block.sync
        def _(sp):
            sp.dma_start(wqkv[:], io["WqkvT"].rearrange("(c p) n -> p c n", p=P)).then_inc(loaded, 16)
            sp.dma_start(bqkv[:], io["bqkv"]).then_inc(loaded, 16)
            sp.dma_start(wproj[:], io["WprojT"].rearrange("(c p) n -> p c n", p=P)).then_inc(loaded, 16)
            sp.dma_start(temp[:], io["temp"].broadcast_to([P, H])).then_inc(loaded, 16)

            def load(g, b, turn):
                if turn is not None:
                    wait(sp, got_rows[b], turn * (16 * K4))
                sp.dma_start(idx[b][:], io["src"][bass.ds(g, 1), :, :].rearrange("a p k -> (a p) k")
                             ).then_inc(idx_loaded[b], 16)
                if turn is not None:
                    wait(sp, et_found, g - 1)
                base = sp.value_load(keep.base[0:1, bass.ds(g, 1)], min_val=0, max_val=NT - 1)
                sp.dma_start(etw[b][:], dram.et[bass.ds(base, WN), :]).then_inc(etw_loaded[b], 16)

            load(0, 0, None)
            load(1, 1, None)
            with sp.Fori(1, G1 // 2) as i:
                for b in range(2):
                    load(i * 2 + b, b, i)
            load(G1, 0, G1 // 2)
            sp.wait_ge(idx_loaded[0], 16 * (G1 // 2 + 1))
            sp.wait_ge(etw_loaded[0], 16 * (G1 // 2 + 1))

        @block.gpsimd
        def _(pool):
            step = Chain(pool, p_step)
            step(pool.memset(mhalf[:], -0.5))

            def gather(b):
                for k in range(K4):
                    pool.indirect_dma_start(out=got[b][:, k, :], out_offset=None, in_=dram.table,
                                            in_offset=bass.IndirectOffsetOnAxis(ap=idx[b][:, k:k + 1], axis=0)
                                            ).then_inc(got_rows[b], 16)

            def inverse_norm(n):
                wait(pool, ss_made, n + 1)
                pool.tensor_tensor(rn[:], ss[:], mhalf[:], ALU.pow).then_inc(rn_made, 1)

            inverse_norm(0)
            pool.wait_ge(idx_loaded[0], 16)
            gather(0)
            pool.wait_ge(idx_loaded[1], 16)
            gather(1)
            with pool.Fori(1, G1 // 2) as i:
                for b in range(2):
                    wait(pool, msg_made, i * 2 + b - 1)
                    wait(pool, idx_loaded[b], i * 16 + 16)
                    gather(b)
                    if b == 0:
                        inverse_norm(i)
            inverse_norm(G1 // 2)

        @block.vector
        def _(v):
            step = Chain(v, v_step)
            v.memset(zero[:], 0.0).then_inc(filled, 1)
            v.memset(keep.accF[:], 0.0)
            v.memset(keep.accD[:], 0.0)
            v.memset(diag[:], 0.0)
            for b in range(2):
                v.memset(msg[b][:, :, TF:MSG], 0.0)
            step(v.memset(tail[:, :, TAIL - 1:TAIL], 1.0))

            def one_hot(g, b, used):
                if used is not None:
                    wait(v, scattered, used)
                v.tensor_tensor(oh[b][:], keep.iota[:].unsqueeze(1).broadcast_to([P, K4, WN]),
                                keep.rel[:, bass.ds(g, 1), :].rearrange("p a k -> p (a k)").unsqueeze(2)
                                .broadcast_to([P, K4, WN]), ALU.is_equal).then_inc(oh_made, 1)

            def logits(g, b, turn):
                wait(v, et_found, g + 1)
                wait(v, got_rows[b], turn * (16 * K4))
                tgt = psE[:, 0:K4 * H].rearrange("p (k h) -> p k h", h=H)
                step(v.tensor_tensor(lb[:], tgt, keep.bound[:].unsqueeze(1).broadcast_to([P, K4, H]), ALU.add))
                step(v.tensor_tensor(lg[:], tgt, keep.ee[:, bass.ds(g * (K4 * H), K4 * H)]
                                     .rearrange("p (k h) -> p k h", h=H), ALU.add))
                step(v.tensor_tensor(lg[:], lg[:], got[b][:, :, C:TF], ALU.add))
                step(v.scalar_tensor_tensor(lb[:], lb[:], 0.2, lb[:], ALU.mult, ALU.max))
                step(v.scalar_tensor_tensor(lg[:], lg[:], 0.2, lg[:], ALU.mult, ALU.max))
                v.tensor_tensor(lg[:], lg[:], lb[:], ALU.subtract).then_inc(logits_made, 1)

            def scale(g, b):
                wait(v, exp_made, g + 1)
                v.tensor_tensor(msg[b][:, :, 0:C].rearrange("p k (h d) -> p k h d", d=D),
                                got[b][:, :, 0:C].rearrange("p k (h d) -> p k h d", d=D),
                                msg[b][:, :, C:TF].unsqueeze(3).broadcast_to([P, K4, H, D]),
                                ALU.mult).then_inc(msg_made, 1)

            def add_window(g):
                base = v.value_load(keep.base[0:1, bass.ds(g, 1)], min_val=0, max_val=NT - 1)
                wait(v, scattered, g + 1)
                to = keep.accF[:, :, bass.ds(base, WN)]
                step(v.tensor_tensor(to, to, psS[:, 0:CB * WN].rearrange("p (c n) -> p c n", c=CB), ALU.add))
                to = keep.accD[:, bass.ds(base, WN)]
                v.tensor_tensor(to, to, psS[:, CB * WN:(CB + 1) * WN], ALU.add).then_inc(added, 1)

            def sum_squares(n, floor):
                wait(v, squared, n + 1)
                step(v.tensor_reduce(ss[:], sq[:].rearrange("p (h d) -> p h d", h=H), AX_X, ALU.add))
                v.tensor_scalar(ss[:], ss[:], floor, None, ALU.max).then_inc(ss_made, 1)

            def features(n, by, done):
                wait(v, rn_made, n + 1)
                if by is not None:
                    step(v.tensor_tensor(rq[:], rn[:], by[:], ALU.mult))
                    by = rq
                else:
                    by = rn
                if done is not None:
                    done()
                vec = psP[:, 0:C].rearrange("p (h d) -> p h d", h=H)
                byb = by[:].unsqueeze(2).broadcast_to([P, H, D])
                step(v.tensor_tensor(dup[:, :, 0:D], vec, byb, ALU.mult))
                step(v.tensor_copy(dup[:, :, D:DUP], dup[:, :, 0:DUP - D]))
                if by is rn:
                    v.tensor_copy(tail[:, :, 16:16 + D], dup[:, :, 0:D])
                    v.tensor_tensor(tail[:, :, 0:16], dup[:, :, 0:16], dup[:, :, 16:32], ALU.mult)
                else:
                    v.tensor_copy(unit[:].rearrange("p (h d) -> p h d", h=H), dup[:, :, 0:D])
                    v.tensor_tensor(far[:].rearrange("p (h d) -> p h d", h=H), dup[:, :, 0:16], dup[:, :, 16:32],
                                    ALU.mult)
                window = bass.AP(dup[:].tensor, 0, [[H * DUP, P], [DUP, H], [1, 16], [1, D]])
                v.tensor_tensor(phi[:], window, dup[:, :, 0:D].unsqueeze(2).broadcast_to([P, H, 16, D]),
                                ALU.mult).then_inc(phi_made, 1)

            def k_turn(t, last):
                g0 = t * 2
                one_hot(g0 + 1, 1, g0 if not isinstance(t, int) or t else None)
                logits(g0, 0, t + 1)
                features(t, None, (lambda: wait(v, k_summed, t)) if not isinstance(t, int) or t else None)
                scale(g0, 0)
                add_window(g0)
                one_hot(g0 + 2, 0, g0 + 1)
                logits(g0 + 1, 1, t + 1)
                scale(g0 + 1, 1)
                sum_squares(t + 1, EPS_N ** 2 if not last else (EPS_N / SC) ** 2)
                add_window(g0 + 1)

            one_hot(0, 0, None)
            sum_squares(0, EPS_N ** 2)
            k_turn(0, False)
            with v.Fori(1, T - 1) as t:
                step.enter(t - 1, 2 * 5 + 2 + 2 + 1)
                k_turn(t, False)
                step.leave(T - 2)
            k_turn(T - 1, True)

            v.wait_ge(k_summed, T)
            lay = [0]

            def laid(ins):
                lay[0] += 1
                ins.then_inc(kv_laid, 1)

            for half in range(CB):
                if half:
                    v.wait_ge(kv_turned, 4)
                v.tensor_scalar(kvt[:, 0:D], acc[half][:, 0:D], 0.5 * SC ** 2, None, ALU.mult)
                laid(v.tensor_scalar(kvt[:, D:512], acc[half][:, D:512], SC ** 2, None, ALU.mult))
                for dg in range(4):
                    v.wait_ge(kv_turned, half * 4 + dg + 1)
                    v.tensor_copy(kv[:, half, dg, :], psU[:, dg % 2 * P:dg % 2 * P + P]).then_inc(kv_copied, 1)
            for half in range(CB):
                for h in range(HALF):
                    ins = v.tensor_scalar(diag[D * h:D * h + D, 16 * (HALF * half + h):16 * (HALF * half + h) + 16],
                                          accT[D * h:D * h + D, half * TAIL:half * TAIL + 16],
                                          SC ** 2, None, ALU.mult)
                laid(ins)
                v.wait_ge(kv_turned, 8 + 2 * half + 1)
                v.tensor_copy(kv16[:, half, :], psU[:, 0:P]).then_inc(kv_copied, 1)
                step(v.memset(diag[:], 0.0))
                for h in range(HALF):
                    ins = v.tensor_scalar(diag[D * h:D * h + D, D * h:D * h + D],
                                          accT[D * h:D * h + D, half * TAIL + 16:half * TAIL + 16 + D],
                                          SC ** 3, None, ALU.mult)
                laid(ins)
                v.wait_ge(kv_turned, 8 + 2 * half + 2)
                v.tensor_copy(kvlin[:, half, :], psU[:, P:2 * P]).then_inc(kv_copied, 1)
                step(v.memset(diag[:], 0.0))
                step(v.memset(gram[:, half, :], 0.0))
                at = CB * TAIL + half * (D + 1)
                for h in range(HALF):
                    v.tensor_scalar(gram[D * h:D * h + D, half, D * h:D * h + D], accT[D * h:D * h + D, at:at + D],
                                    0.5 * SC ** 2 / N, None, ALU.mult)
                v.tensor_scalar(ksum[:, half:half + 1], accT[:, at + D:at + D + 1], SC ** 3 / N, None, ALU.mult)
                laid(v.tensor_scalar(vsum[:, half:half + 1], accT[:, (half + 1) * TAIL - 1:(half + 1) * TAIL],
                                     SC ** 4, None, ALU.mult))
            step(v.tensor_scalar(temp[:], temp[:], SC, None, ALU.mult))

            def numerator(n):
                wait(v, y_summed, n + 1)
                for half in range(CB):
                    last = v.scalar_tensor_tensor(wq[:, half, :], psU[:, half * P:half * P + P],
                                                  ksum[:, half:half + 1], phiT[:, 33 + half, :], ALU.add, ALU.mult)
                last.then_inc(wq_made, 1)

            def quotient(n):
                wait(v, norm_summed, n + 1)
                step(v.tensor_scalar(rec[:], psU[:, C:2 * C].rearrange("p (c n) -> p c n", c=CB), SC ** 4, None,
                                     ALU.add))
                step(v.reciprocal(rec[:], rec[:]))
                for half in range(CB):
                    last = v.scalar_tensor_tensor(mixT[:, half, :], accT[:, half * P:half * P + P],
                                                  vsum[:, half:half + 1], rec[:, half, :], ALU.add, ALU.mult)
                last.then_inc(mix_made, 1)

            def add_mix(n):
                wait(v, out_summed, n + 1)
                to = keep.x[:, bass.ds(n, 1), :].rearrange("p a c -> p (a c)")
                v.tensor_tensor(to, to, psU[:, 0:C], ALU.add).then_inc(x_added, 1)

            def q_turn(t):
                g0 = t * 2 + 2 * T
                one_hot(g0 + 1, 1, g0)
                logits(g0, 0, t + T + 1)
                features(t + T, temp, (lambda: wait(v, phi_turned, t * 9)) if not isinstance(t, int) or t else None)
                scale(g0, 0)
                add_window(g0)
                one_hot(g0 + 2, 0, g0 + 1)
                logits(g0 + 1, 1, t + T + 1)
                numerator(t)
                scale(g0 + 1, 1)
                quotient(t)
                add_window(g0 + 1)
                add_mix(t)
                sum_squares(t + T + 1, (EPS_N / SC) ** 2)

            q_turn(0)
            with v.Fori(1, T - 1) as t:
                step.enter(t - 1, 2 * 5 + 2 + 1 + 2 + 2 + 1)
                q_turn(t)
                step.leave(T - 2)
            features(2 * T - 1, temp, lambda: wait(v, phi_turned, (T - 1) * 9))
            numerator(T - 1)
            quotient(T - 1)
            add_mix(T - 1)

        @block.scalar
        def _(act):
            def turn_back(g, b, used):
                wait(act, oh_turned, g + 1)
                if used is not None:
                    wait(act, et_found, used)
                act.copy(ohT[b][:], psT[:].rearrange("p (k n) -> p k n", k=K4)).then_inc(ohT_made, 1)

            def exponent(g, b, used):
                wait(act, logits_made, g + 1)
                if used is not None:
                    wait(act, scattered, used)
                act.activation(msg[b][:, :, C:TF], lg[:], ACT.Exp).then_inc(exp_made, 1)

            def stage(n, t, before):
                if before is not None:
                    wait(act, projected, before)
                act.copy(vs[:], keep.vrow[:, bass.ds(t * P, P)])
                act.copy(xs[:], keep.xT[:, :, bass.ds(t * P, P)]).then_inc(xs_made, 1)

            def square(n, key, used):
                wait(act, projected, n + 1)
                if key:
                    if used is not None:
                        wait(act, k_summed, used)
                    act.mul(vt[:], psP[:, C:2 * C], 1.0 / N)
                if not (isinstance(n, int) and n == 0):
                    wait(act, ss_made, n)
                act.activation(sq[:], psP[:, 0:C], ACT.Square).then_inc(squared, 1)

            def copies(t):
                for r in range(9):
                    wait(act, phi_turned, t * 9 + r + 1)
                    w = 4 if r < 8 else 3
                    act.copy(phiT[:, 4 * r:4 * r + w, :],
                             acc[r % 2][:, 0:w * P].rearrange("p (k n) -> p k n", k=w)).then_inc(phiT_made, 1)

            def k_turn(t, last):
                g0 = t * 2
                first = isinstance(t, int) and t == 0
                turn_back(g0 + 1, 1, None if first else g0)
                exponent(g0, 0, None if first else g0 - 1)
                turn_back(g0 + 2, 0, g0 + 1)
                exponent(g0 + 1, 1, None if first else g0)
                if not last:
                    square(t + 1, True, t + 1)
                    stage(t + 2, t + 2, t + 2)
                else:
                    square(T, False, None)
                    stage(T + 1, 1, T + 1)

            stage(0, 0, None)
            turn_back(0, 0, None)
            square(0, True, None)
            stage(1, 1, 1)
            k_turn(0, False)
            with act.Fori(1, T - 2) as t:
                k_turn(t, False)
            g0 = (T - 2) * 2
            turn_back(g0 + 1, 1, g0)
            exponent(g0, 0, g0 - 1)
            turn_back(g0 + 2, 0, g0 + 1)
            exponent(g0 + 1, 1, g0)
            square(T - 1, True, T - 1)
            stage(T, 0, T)
            k_turn(T - 1, True)

            def q_turn(t):
                g0 = t * 2 + 2 * T
                turn_back(g0 + 1, 1, g0)
                exponent(g0, 0, g0 - 1)
                copies(t)
                turn_back(g0 + 2, 0, g0 + 1)
                exponent(g0 + 1, 1, g0)
                square(t + T + 1, False, None)

            with act.Fori(0, T - 2) as t:
                q_turn(t)
                stage(t + T + 2, t + 2, t + T + 2)
            q_turn(T - 2)
            copies(T - 1)

        @block.tensor
        def _(pe):
            pe.wait_ge(loaded, 64)

            def turn(g, b):
                wait(pe, oh_made, g + 1)
                if not (isinstance(g, int) and g == 0):
                    wait(pe, ohT_made, g)
                for k in range(K4):
                    last = pe.transpose(psT[:, k * P:k * P + P], oh[b][:, k, :], keep.ident[:])
                last.then_inc(oh_turned, 1)

            def find(g, b, turns):
                wait(pe, ohT_made, g + 1)
                wait(pe, etw_loaded[b], turns * 16)
                if not (isinstance(g, int) and g == 0):
                    wait(pe, logits_made, g)
                for k in range(K4):
                    for part in range(3):
                        last = pe.matmul(psE[:, k * H:k * H + H], ohT[b][:, k, :], etw[b][:, part * H:part * H + H],
                                         start=(part == 0), stop=(part == 2))
                last.then_inc(et_found, 1)

            def scatter(g, b):
                wait(pe, msg_made, g + 1)
                if not (isinstance(g, int) and g == 0):
                    wait(pe, added, g)
                for c in range(CB):
                    for k in range(K4):
                        pe.matmul(psS[:, c * WN:c * WN + WN], msg[b][:, k, c * P:c * P + P], oh[b][:, k, :],
                                  start=(k == 0), stop=(k == K4 - 1))
                for k in range(K4):
                    last = pe.matmul(psS[32 * k:32 * k + 32, CB * WN:CB * WN + WN], msg[b][:, k, C:MSG], oh[b][:, k, :],
                                     start=True, stop=True)
                last.then_inc(scattered, 1)

            def project(n, key):
                wait(pe, xs_made, n + 1)
                lo, hi = (C, 3 * C) if key else (0, C)
                for c in range(CB):
                    pe.matmul(psP[:, 0:hi - lo], xs[:, c, :], wqkv[:, c, lo:hi], start=(c == 0), stop=False)
                pe.matmul(psP[:, 0:hi - lo], vs[:], bqkv[:, lo:hi], start=False, stop=True).then_inc(projected, 1)

            def sum_keys(t, last_tile):
                wait(pe, phi_made, t + 1)
                for half in range(CB):
                    for h in range(HALF):
                        hh = HALF * half + h
                        rows = slice(D * h, D * h + D)
                        pe.matmul(acc[half][rows, :], vt[:, hh * D:hh * D + D],
                                  phi[:, hh, :, :].rearrange("p d i -> p (d i)"),
                                  start=False, stop=last_tile, skip_group_check=True)
                    for h in range(HALF):
                        hh = HALF * half + h
                        rows = slice(D * h, D * h + D)
                        pe.matmul(accT[rows, half * TAIL:(half + 1) * TAIL], vt[:, hh * D:hh * D + D], tail[:, hh, :],
                                  start=False, stop=last_tile, skip_group_check=True)
                    for h in range(HALF):
                        hh = HALF * half + h
                        rows = slice(D * h, D * h + D)
                        at = CB * TAIL + half * (D + 1)
                        last = pe.matmul(accT[rows, at:at + D + 1], tail[:, hh, 16:16 + D], tail[:, hh, 16:TAIL],
                                         start=False, stop=last_tile, skip_group_check=True)
                last.then_inc(k_summed, 1)

            def k_turn(t, last):
                g0 = t * 2
                turn(g0 + 1, 1)
                find(g0 + 1, 1, t + 1)
                sum_keys(t, last)
                scatter(g0, 0)
                turn(g0 + 2, 0)
                project(t + 1 if not last else T, not last)
                find(g0 + 2, 0, t + 2)
                scatter(g0 + 1, 1)

            pe.wait_ge(filled, 1)
            for bank in (acc[0], acc[1], accT):
                pe.matmul(bank[:], zero[:, 0:P], zero[:], start=True, stop=False, skip_group_check=True)
            turn(0, 0)
            project(0, True)
            find(0, 0, 1)
            k_turn(0, False)
            with pe.Fori(1, T - 1) as t:
                k_turn(t, False)
            k_turn(T - 1, True)

            for half in range(CB):
                pe.wait_ge(kv_laid, half + 1)
                for dg in range(4):
                    n = half * 4 + dg
                    if n >= 1:
                        pe.wait_ge(kv_copied, n)
                    pe.transpose(psU[:, dg % 2 * P:dg % 2 * P + P], kvt[:, dg * P:dg * P + P],
                                 keep.ident[:]).then_inc(kv_turned, 1)
            for half in range(CB):
                for j in range(2):
                    pe.wait_ge(kv_laid, CB + 3 * half + j + 1)
                    pe.wait_ge(kv_copied, 8 + 2 * half + j)
                    pe.transpose(psU[:, j * P:j * P + P], diag[:], keep.ident[:]).then_inc(kv_turned, 1)
            pe.wait_ge(kv_laid, CB + 3 * CB)

            def turn_features(t):
                wait(pe, phi_made, t + T + 1)
                for r in range(9):
                    if r >= 2:
                        wait(pe, phiT_made, t * 9 + r - 1)
                    for j in range(4 if r < 8 else 3):
                        if r < 8:
                            block_in = phi[:, r, 4 * j:4 * j + 4, :].rearrange("p d i -> p (d i)")
                        elif j == 0:
                            block_in = far[:]
                        else:
                            block_in = unit[:, (j - 1) * P:j * P]
                        last = pe.transpose(acc[r % 2][:, j * P:j * P + P], block_in, keep.ident[:])
                    last.then_inc(phi_turned, 1)

            def values(t):
                wait(pe, phiT_made, t * 9 + 9)
                if not (isinstance(t, int) and t == 0):
                    wait(pe, x_added, t)
                for half in range(CB):
                    cols = slice(half * P, half * P + P)
                    pe.matmul(accT[:, cols], kv16[:, half, :], phiT[:, 32, :], start=True, stop=False,
                              skip_group_check=True)
                    pe.matmul(accT[:, cols], kvlin[:, half, :], phiT[:, 33 + half, :], start=False, stop=False,
                              skip_group_check=True)
                    for dg in range(4):
                        for h in range(HALF):
                            pe.matmul(accT[D * h:D * h + D, cols], kv[:, half, dg, D * h:D * h + D],
                                      phiT[:, 4 * (HALF * half + h) + dg, :], start=False, stop=(dg == 3),
                                      skip_group_check=True)
                for half in range(CB):
                    last = pe.matmul(psU[:, half * P:half * P + P], gram[:, half, :], phiT[:, 33 + half, :],
                                     start=True, stop=True)
                last.then_inc(y_summed, 1)

            def norms(t):
                wait(pe, wq_made, t + 1)
                for half in range(CB):
                    last = pe.matmul(psU[:, C + half * P:C + half * P + P], keep.ones[:], wq[:, half, :],
                                     start=True, stop=True)
                last.then_inc(norm_summed, 1)

            def out(t):
                wait(pe, mix_made, t + 1)
                for half in range(CB):
                    last = pe.matmul(psU[:, 0:C], mixT[:, half, :], wproj[:, half, :], start=(half == 0),
                                     stop=(half == CB - 1))
                last.then_inc(out_summed, 1)

            def q_turn(t):
                g0 = t * 2 + 2 * T
                turn(g0 + 1, 1)
                find(g0 + 1, 1, t + T + 1)
                turn_features(t)
                scatter(g0, 0)
                turn(g0 + 2, 0)
                values(t)
                find(g0 + 2, 0, t + T + 2)
                norms(t)
                scatter(g0 + 1, 1)
                out(t)
                project(t + T + 1, False)

            q_turn(0)
            with pe.Fori(1, T - 1) as t:
                q_turn(t)
            turn_features(T - 1)
            values(T - 1)
            norms(T - 1)
            out(T - 1)


def combine(nc, io, keep, dram):
    with ExitStack() as ctx:
        def sb(name, shape, dt=F32):
            return ctx.enter_context(nc.sbuf_tensor(name, shape, dt))

        def psum(name):
            return ctx.enter_context(nc.psum_tensor(name, [P, 512], F32))

        def sem(name):
            return ctx.enter_context(nc.semaphore(name))

        sums = [sb(f"sums{b}", [P, CB, P]) for b in range(2)]
        dens = [sb(f"dens{b}", [P, P]) for b in range(2)]
        rden = sb("rden", [P, H])
        part = sb("part", [P, C])
        bias, bias2 = sb("bias", [P, C]), sb("bias2", [P, C])
        stats, agg = sb("stats_c", [P, 6]), sb("agg_c", [P, 2])
        mv = sb("mv_c", [P, T, 2])
        vare, rstd, half = sb("vare_c", [P, T]), sb("rstd_c", [P, T]), sb("half_c", [P, T])
        xn = [sb(f"xn_c{b}", [P, C]) for b in range(2)]
        xt = [sb(f"xt_c{b}", [P, CB, P]) for b in range(2)]
        wg = sb("wg", [P, CB, HC + 2 * H2])
        as_, ad = sb("as_", [P, HC]), sb("ad", [P, HC])
        prod = sb("prod_c", [P, CB, HC])
        amax = sb("amax", [P, H2])
        psG = [psum(f"psG{b}") for b in range(2)]
        psX = [psum(f"psXc{b}") for b in range(2)]
        psH = [psum(f"psH{b}") for b in range(2)]
        loaded, v_step, p_step = sem("loaded_c"), sem("v_step_c"), sem("p_step_c")
        staged, turned, joined = sem("staged"), sem("turned"), sem("joined")
        var_made, rstd_made = sem("var_made_c"), sem("rstd_made_c")
        xn_made, xn_turned, xt_copied, h_summed, h_copied = (sem("xn_made_c"), sem("xn_turned_c"), sem("xt_copied_c"),
                                                             sem("h_summed"), sem("h_copied"))
        weights_made, amax_made, stored, amax_all = (sem("weights_made_c"), sem("amax_made"), sem("stored_c"),
                                                     sem("amax_all"))
        block = ctx.enter_context(nc.Block())

        @block.sync
        def _(sp):
            sp.dma_start(bias[:], io["bias"].broadcast_to([P, C])).then_inc(loaded, 16)
            sp.dma_start(bias2[:], io["bproj"].broadcast_to([P, C])).then_inc(loaded, 16)
            sp.dma_start(wg[:, :, 0:HC], io["W_gat"].rearrange("(c p) n -> p c n", p=P)).then_inc(loaded, 16)
            sp.dma_start(as_[:], io["att_src"].broadcast_to([P, HC])).then_inc(loaded, 16)
            sp.dma_start(ad[:], io["att_dst"].broadcast_to([P, HC])).then_inc(loaded, 16)
            sp.wait_ge(h_copied, T)
            sp.dma_start(dram.source.rearrange("(t p) c -> p t c", p=P), keep.h[:, :, 0:R2]).then_inc(stored, 16)
            sp.dma_start(dram.target.rearrange("(t p) c -> p t c", p=P), keep.h[:, :, R2:R2 + H2]).then_inc(stored, 16)
            sp.wait_ge(stored, 32)

        @block.gpsimd
        def _(pool):
            step = Chain(pool, p_step)
            step(pool.memset(half[:], -0.5))
            pool.wait_ge(var_made, 1)
            pool.tensor_tensor(rstd[:], vare[:], half[:], ALU.pow).then_inc(rstd_made, 1)
            pool.wait_ge(amax_made, 1)
            pool.partition_all_reduce(keep.amax[:], amax[:], P, RMAX).then_inc(amax_all, 1)

        @block.scalar
        def _(act):
            def stage(t, b, first):
                if not first:
                    wait(act, turned, t - 1)
                act.copy(sums[b][:], keep.accF[:, :, bass.ds(t * P, P)])
                act.copy(dens[b][:], keep.accD[:, bass.ds(t * P, P)]).then_inc(staged, 1)

            stage(0, 0, True)
            stage(1, 1, True)
            with act.Fori(1, T // 2) as i:
                for b in range(2):
                    stage(i * 2 + b, b, False)
            stage(T - 1, 0, False)

            def tile(t, b, first):
                wait(act, xn_turned, t + 1)
                xv = psX[b][:, 0:C].rearrange("p (c n) -> p c n", c=CB)
                act.copy(keep.xT[:, :, bass.ds(t * P, P)], xv)
                if not first:
                    wait(act, h_summed, t - 1)
                act.copy(xt[b][:], xv).then_inc(xt_copied, 1)
                wait(act, h_summed, t + 1)
                act.copy(keep.h[:, bass.ds(t, 1), :].rearrange("p a c -> p (a c)"),
                         psH[b][:, 0:HC + 2 * H2]).then_inc(h_copied, 1)

            tile(0, 0, True)
            tile(1, 1, True)
            with act.Fori(1, T // 2) as i:
                for b in range(2):
                    tile(i * 2 + b, b, False)
            tile(T - 1, 0, False)

        @block.vector
        def _(v):
            step = Chain(v, v_step)
            v.wait_ge(loaded, 80)
            step(v.tensor_tensor(bias[:], bias[:], bias2[:], ALU.add))
            for n, vec in enumerate((as_, ad)):
                step(v.tensor_tensor(prod[:], wg[:, :, 0:HC], vec[:].unsqueeze(1).broadcast_to([P, CB, HC]), ALU.mult))
                v.tensor_reduce(wg[:, :, HC + n * H2:HC + n * H2 + H2],
                                prod[:].rearrange("p c (h x) -> p c h x", h=H2), AX_X, ALU.add
                                ).then_inc(weights_made, 1)
                v.wait_ge(weights_made, n + 1)

            def join(t, b):
                wait(v, turned, t + 1)
                xr = keep.x[:, bass.ds(t, 1), :].rearrange("p a c -> p (a c)")
                step(v.tensor_scalar(rden[:], psG[b][:, C:C + H], TINY, None, ALU.max))
                step(v.reciprocal(rden[:], rden[:]))
                step(v.tensor_tensor(part[:].rearrange("p (h d) -> p h d", h=H),
                                     psG[b][:, 0:C].rearrange("p (h d) -> p h d", h=H),
                                     rden[:].unsqueeze(2).broadcast_to([P, H, D]), ALU.mult))
                step(v.tensor_tensor(part[:], part[:], bias[:], ALU.add))
                step(v.tensor_tensor(xr, xr, part[:], ALU.add))
                step(v.bn_stats(stats[:], xr))
                step(v.bn_aggr(agg[:], stats[:]))
                v.tensor_copy(mv[:, bass.ds(t, 1), :].rearrange("p a c -> p (a c)"), agg[:]).then_inc(joined, 1)
                wait(v, joined, t + 1)

            with v.Fori(0, T // 2) as i:
                step.enter(i, 14)
                for b in range(2):
                    join(i * 2 + b, b)
                step.leave(T // 2)
            join(T - 1, 0)
            v.tensor_scalar(vare[:], mv[:, :, 1], EPS_LN, None, ALU.add).then_inc(var_made, 1)
            v.wait_ge(rstd_made, 1)

            def norm(t, b, first):
                if not first:
                    wait(v, xn_turned, t - 1)
                v.tensor_scalar(xn[b][:], keep.x[:, bass.ds(t, 1), :].rearrange("p a c -> p (a c)"),
                                mv[:, bass.ds(t, 1), 0:1].rearrange("p a c -> p (a c)"), rstd[:, bass.ds(t, 1)],
                                ALU.subtract, ALU.mult).then_inc(xn_made, 1)

            norm(0, 0, True)
            norm(1, 1, True)
            with v.Fori(1, T // 2) as i:
                for b in range(2):
                    norm(i * 2 + b, b, False)
            norm(T - 1, 0, False)
            v.wait_ge(h_copied, T)
            v.tensor_reduce(amax[:], keep.h[:, :, HC:R2].rearrange("p t h -> p h t"), AX_X, ALU.max
                            ).then_inc(amax_made, 1)
            v.wait_ge(amax_all, 1)

        @block.tensor
        def _(pe):
            def turn(t, b, first):
                wait(pe, staged, t + 1)
                if not first:
                    wait(pe, joined, t - 1)
                for c in range(CB):
                    pe.transpose(psG[b][:, c * P:c * P + P], sums[b][:, c, :], keep.ident[:])
                pe.matmul(psG[b][:, C:C + H], dens[b][:], keep.sel8[:], start=True, stop=True).then_inc(turned, 1)

            turn(0, 0, True)
            turn(1, 1, True)
            with pe.Fori(1, T // 2) as i:
                for b in range(2):
                    turn(i * 2 + b, b, False)
            turn(T - 1, 0, False)
            pe.wait_ge(weights_made, 2)

            def tile(t, b, first):
                wait(pe, xn_made, t + 1)
                if not first:
                    wait(pe, xt_copied, t - 1)
                for c in range(CB):
                    last = pe.transpose(psX[b][:, c * P:c * P + P], xn[b][:, c * P:c * P + P], keep.ident[:])
                last.then_inc(xn_turned, 1)
                wait(pe, xt_copied, t + 1)
                if not first:
                    wait(pe, h_copied, t - 1)
                for c in range(CB):
                    last = pe.matmul(psH[b][:, 0:HC + 2 * H2], xt[b][:, c, :], wg[:, c, :], start=(c == 0),
                                     stop=(c == CB - 1))
                last.then_inc(h_summed, 1)

            tile(0, 0, True)
            tile(1, 1, True)
            with pe.Fori(1, T // 2) as i:
                for b in range(2):
                    tile(i * 2 + b, b, False)
            tile(T - 1, 0, False)


def experts(nc, io, keep, dram):
    with ExitStack() as ctx:
        def sb(name, shape, dt=F32):
            return ctx.enter_context(nc.sbuf_tensor(name, shape, dt))

        def psum(name):
            return ctx.enter_context(nc.psum_tensor(name, [P, 512], F32))

        def sem(name):
            return ctx.enter_context(nc.semaphore(name))

        w1 = sb("w1", [P, X, CB, HID])
        b1 = sb("b1", [P, X * HB])
        w2 = sb("w2", [P, X, HB, C])
        b2 = sb("b2", [P, X, C])
        hid = [sb(f"hid{b}", [P, HB, P]) for b in range(2)]
        y = [sb(f"y{b}", [P, X, C]) for b in range(2)]
        ei = sb("ei", [P, 2, G2 * K4], I32)
        hi_i, lo_i = sb("hi_i", [P, G2 * K4], I32), sb("lo_i", [P, G2 * K4], I32)
        hi, lo = sb("hi", [P, G2 * K4]), sb("lo", [P, G2 * K4])
        idx = [sb(f"idx_d{b}", [P, 2 * K4], I32) for b in range(2)]
        src = [sb(f"src{b}", [P, K4, R2]) for b in range(2)]
        tgt = [sb(f"tgt{b}", [P, K4, H2]) for b in range(2)]
        oh_lo = [sb(f"oh_lo{b}", [P, K4, P]) for b in range(2)]
        oh_hi = sb("oh_hi", [P, K4, T])
        lg = sb("lg_d", [P, K4, H2])
        lb = sb("lb_d", [P, K4, H2])
        val = sb("val", [P, K4, R2])
        rows = [sb(f"rows{b}", [P, K4, T * R2]) for b in range(2)]
        zero = sb("zero_d", [P, 512])
        psA = psum("psA")
        ps1 = [psum(f"ps1{b}") for b in range(2)]
        ps2 = [psum(f"ps2{b}") for b in range(2)]

        loaded, split_made, v_step, filled = sem("loaded_d"), sem("split_made"), sem("v_step_d"), sem("filled_d")
        idx_loaded = [sem(f"idx_loaded_d{b}") for b in range(2)]
        found = [sem(f"found{b}") for b in range(2)]
        lg_made, ex_made, rows_made, rows_summed = sem("lg_made"), sem("ex_made"), sem("rows_made"), sem("rows_summed")
        taken = sem("taken")
        up_done, act_done, down_done, y_made = sem("up_done"), sem("act_done"), sem("down_done"), sem("y_made")
        y_stored = [sem(f"y_stored{b}") for b in range(2)]
        block = ctx.enter_context(nc.Block())

        @block.sync
        def _(sp):
            sp.dma_start(ei[:], io["edges2"]).then_inc(loaded, 16)
            sp.dma_start(w1[:], io["W1"].rearrange("x (c p) n -> p x c n", p=P)).then_inc(loaded, 16)
            sp.dma_start(w2[:], io["W2"].rearrange("x (c p) n -> p x c n", p=P)).then_inc(loaded, 16)
            sp.dma_start(b1[:], io["b1"]).then_inc(loaded, 16)
            sp.dma_start(b2[:].rearrange("p x c -> p (x c)"), io["b2"].broadcast_to([P, X * C])).then_inc(loaded, 16)

            def load(g, b, turn):
                if turn is not None:
                    wait(sp, found[b], turn * (32 * K4))
                sp.dma_start(idx[b][:], io["idx2"][bass.ds(g, 1), :, :].rearrange("a p k -> (a p) k")
                             ).then_inc(idx_loaded[b], 16)

            def store(t, b):
                wait(sp, y_made, t * X + X)
                sp.dma_start(dram.y[bass.ds(t * P, P), :], y[b][:].rearrange("p x c -> p (x c)")
                             ).then_inc(y_stored[b], 16)

            load(0, 0, None)
            load(1, 1, None)
            with sp.Fori(0, T // 2) as i:
                for b in range(2):
                    for u in range(2):
                        load(i * 4 + 2 * b + u + 2, u, i * 2 + b + 1)
                    store(i * 2 + b, b)
            with sp.Fori(T // 2 * 2, G2 // 2 - 1) as j:
                for u in range(2):
                    load(j * 2 + 2 + u, u, j + 1)
            store(T - 1, 0)
            for b in range(2):
                sp.wait_ge(y_stored[b], 16 * ((T + 1 - b) // 2))

        @block.gpsimd
        def _(pool):
            def gather(b):
                for k in range(K4):
                    for (to, table, col) in ((src, dram.source, k), (tgt, dram.target, K4 + k)):
                        pool.indirect_dma_start(out=to[b][:, k, :], out_offset=None, in_=table,
                                                in_offset=bass.IndirectOffsetOnAxis(ap=idx[b][:, col:col + 1], axis=0)
                                                ).then_inc(found[b], 16)

            for b in range(2):
                pool.wait_ge(idx_loaded[b], 16)
                gather(b)
            with pool.Fori(1, G2 // 2) as i:
                for b in range(2):
                    wait(pool, taken, i * 2 + b - 1)
                    wait(pool, idx_loaded[b], i * 16 + 16)
                    gather(b)

        @block.vector
        def _(v):
            step = Chain(v, v_step)
            v.memset(zero[:], 0.0).then_inc(filled, 1)
            v.wait_ge(loaded, 80)
            v.tensor_scalar(hi_i[:], ei[:, 1, :], 7, None, ALU.arith_shift_right)
            step(v.tensor_scalar(lo_i[:], ei[:, 1, :], P - 1, None, ALU.bitwise_and))
            v.tensor_copy(hi[:], hi_i[:])
            step(v.tensor_copy(lo[:], lo_i[:]))

            def group(g, b, first, turn):
                cols = bass.ds(g * K4, K4)
                if not first:
                    wait(v, rows_summed, g - 1)
                v.tensor_tensor(oh_lo[b][:], keep.iota[:].unsqueeze(1).broadcast_to([P, K4, P]),
                                lo[:, cols].unsqueeze(2).broadcast_to([P, K4, P]), ALU.is_equal)
                v.tensor_tensor(oh_hi[:], keep.iota[:, 0:T].unsqueeze(1).broadcast_to([P, K4, T]),
                                hi[:, cols].unsqueeze(2).broadcast_to([P, K4, T]), ALU.is_equal)
                wait(v, found[b], turn * (32 * K4))
                step(v.tensor_tensor(lg[:], src[b][:, :, HC:R2], tgt[b][:], ALU.add))
                step(v.tensor_tensor(lb[:], tgt[b][:], keep.amax[:].unsqueeze(1).broadcast_to([P, K4, H2]), ALU.add))
                step(v.scalar_tensor_tensor(lg[:], lg[:], 0.2, lg[:], ALU.mult, ALU.max))
                step(v.scalar_tensor_tensor(lb[:], lb[:], 0.2, lb[:], ALU.mult, ALU.max))
                v.tensor_tensor(lg[:], lg[:], lb[:], ALU.subtract).then_inc(lg_made, 1)
                wait(v, ex_made, g + 1)
                v.tensor_tensor(val[:, :, 0:HC].rearrange("p k (h x) -> p k h x", x=X),
                                src[b][:, :, 0:HC].rearrange("p k (h x) -> p k h x", x=X),
                                val[:, :, HC:R2].unsqueeze(3).broadcast_to([P, K4, H2, X]), ALU.mult
                                ).then_inc(taken, 1)
                wait(v, taken, g + 1)
                v.tensor_tensor(rows[b][:].rearrange("p k (t r) -> p k t r", r=R2),
                                oh_hi[:].unsqueeze(3).broadcast_to([P, K4, T, R2]),
                                val[:].unsqueeze(2).broadcast_to([P, K4, T, R2]), ALU.mult).then_inc(rows_made, 1)
                wait(v, rows_made, g + 1)

            def bias(t, b, stored, part):
                if stored is not None:
                    wait(v, y_stored[b], stored)
                for x in part:
                    wait(v, down_done, t * X + x + 1)
                    v.tensor_tensor(y[b][:, x, :], ps2[x % 2][:, 0:C], b2[:, x, :], ALU.add).then_inc(y_made, 1)

            def tile(t, b, g0, first, turn, stored):
                group(g0, 0, first, turn)
                bias(t, b, stored, (0, 1))
                group(g0 + 1, 1, first, turn)
                bias(t, b, stored, (2, 3))

            tile(0, 0, 0, True, 1, None)
            tile(1, 1, 2, False, 2, None)
            with v.Fori(1, T // 2) as i:
                step.enter(i - 1, 16)
                for b in range(2):
                    tile(i * 2 + b, b, i * 4 + 2 * b, False, i * 2 + b + 1, i * 16)
                step.leave(T // 2 - 1)
            tile(T - 1, 0, 2 * T - 2, False, T, T // 2 * 16)
            with v.Fori(T, G2 // 2) as i:
                step.enter(i - T, 8)
                for u in range(2):
                    group(i * 2 + u, u, False, i + 1)
                step.leave(G2 // 2 - T)
            v.wait_ge(rows_summed, G2 + 1)
            v.tensor_copy(keep.agg[:].rearrange("p t r -> p (t r)"), psA[:, 0:T * R2])

        @block.scalar
        def _(act):
            def exponent(g):
                wait(act, lg_made, g + 1)
                if not (isinstance(g, int) and g == 0):
                    wait(act, rows_made, g)
                act.activation(val[:, :, HC:R2], lg[:], ACT.Exp).then_inc(ex_made, 1)

            def gelu(t, x):
                wait(act, up_done, t * X + x + 1)
                if not (isinstance(t, int) and t == 0 and x < 2):
                    wait(act, down_done, t * X + x - 1)
                for j in range(HB):
                    ins = act.activation(hid[x % 2][:, j, :], ps1[x % 2][:, j * P:j * P + P], ACT.Gelu,
                                         bias=b1[:, x * HB + j:x * HB + j + 1])
                ins.then_inc(act_done, 1)

            def tile(t):
                gelu(t, 0)
                exponent(t * 2)
                gelu(t, 1)
                gelu(t, 2)
                exponent(t * 2 + 1)
                gelu(t, 3)

            act.wait_ge(loaded, 80)
            tile(0)
            with act.Fori(1, T) as t:
                tile(t)
            with act.Fori(T * 2, G2) as g:
                exponent(g)

        @block.tensor
        def _(pe):
            pe.wait_ge(filled, 1)
            pe.wait_ge(loaded, 80)
            pe.matmul(psA[:, 0:T * R2], zero[:, 0:P], zero[:, 0:T * R2], start=True, stop=False,
                      skip_group_check=True)

            def add_rows(g, b):
                wait(pe, rows_made, g + 1)
                for k in range(K4):
                    last = pe.matmul(psA[:, 0:T * R2], oh_lo[b][:, k, :], rows[b][:, k, :], start=False, stop=False,
                                     skip_group_check=True)
                last.then_inc(rows_summed, 1)

            def up(t, x):
                if not (isinstance(t, int) and t == 0 and x < 2):
                    wait(pe, act_done, t * X + x - 1)
                for j in range(HB):
                    for c in range(CB):
                        last = pe.matmul(ps1[x % 2][:, j * P:j * P + P], w1[:, x, c, j * P:j * P + P],
                                         keep.xT[:, c, bass.ds(t * P, P)], start=(c == 0), stop=(c == CB - 1))
                last.then_inc(up_done, 1)

            def down(t, x):
                wait(pe, act_done, t * X + x + 1)
                if not (isinstance(t, int) and t == 0 and x < 2):
                    wait(pe, y_made, t * X + x - 1)
                for j in range(HB):
                    last = pe.matmul(ps2[x % 2][:, 0:C], hid[x % 2][:, j, :], w2[:, x, j, :], start=(j == 0),
                                     stop=(j == HB - 1))
                last.then_inc(down_done, 1)

            def tile(t):
                up(t, 0)
                up(t, 1)
                down(t, 0)
                up(t, 2)
                down(t, 1)
                add_rows(t * 2, 0)
                up(t, 3)
                down(t, 2)
                down(t, 3)
                add_rows(t * 2 + 1, 1)

            tile(0)
            with pe.Fori(1, T) as t:
                tile(t)
            with pe.Fori(T, G2 // 2) as i:
                for u in range(2):
                    add_rows(i * 2 + u, u)
            pe.matmul(psA[:, 0:T * R2], zero[:, 0:P], zero[:, 0:T * R2], start=False, stop=True,
                      skip_group_check=True).then_inc(rows_summed, 1)


def route(nc, io, keep, dram):
    with ExitStack() as ctx:
        def sb(name, shape, dt=F32):
            return ctx.enter_context(nc.sbuf_tensor(name, shape, dt))

        def sem(name):
            return ctx.enter_context(nc.semaphore(name))

        bg, gam, bet = sb("bg", [P, HC]), sb("gam", [P, HC]), sb("bet", [P, HC])
        lg, lb, ex = sb("lg_e", [P, T, H2]), sb("lb_e", [P, T, H2]), sb("ex_e", [P, T, H2])
        own = sb("own", [P, T, HC])
        num, sq = sb("num", [P, T, HC]), sb("sq_e", [P, T, HC])
        den = sb("den", [P, T, H2])
        mean, var, rstd, half = sb("mean", [P, T]), sb("var", [P, T]), sb("rstd_e", [P, T]), sb("half_e", [P, T])
        sc, rank, beat = sb("sc", [P, T, X]), sb("rank", [P, T, X]), sb("beat", [P, T])
        top, gate, total = sb("top", [P, T]), sb("gate", [P, T, X]), sb("total", [P, T])
        y = [sb(f"y_e{b}", [P, X, C]) for b in range(2)]
        loaded, v_step, ex_in, ex_out = sem("loaded_e"), sem("v_step_e"), sem("ex_in"), sem("ex_out")
        half_made, var_made, rstd_made = sem("half_made"), sem("var_made_e"), sem("rstd_made_e")
        y_loaded = [sem(f"y_loaded{b}") for b in range(2)]
        summed, stored = sem("summed"), sem("stored_e")
        block = ctx.enter_context(nc.Block())

        @block.sync
        def _(sp):
            for to, name in ((bg, "b_gat"), (gam, "ln_gamma"), (bet, "ln_beta")):
                sp.dma_start(to[:], io[name].broadcast_to([P, HC])).then_inc(loaded, 16)

            def load(t, b, first):
                if not first:
                    wait(sp, summed, t - 1)
                sp.dma_start(y[b][:].rearrange("p x c -> p (x c)"), dram.y[bass.ds(t * P, P), :]
                             ).then_inc(y_loaded[b], 16)

            def store(t):
                wait(sp, summed, t + 1)
                sp.dma_start(io["out"][bass.ds(t * P, P), :],
                             keep.x[:, bass.ds(t, 1), :].rearrange("p a c -> p (a c)")).then_inc(stored, 16)

            load(0, 0, True)
            load(1, 1, True)
            with sp.Fori(0, T // 2 - 1) as i:
                for b in range(2):
                    store(i * 2 + b)
                    load(i * 2 + b + 2, b, False)
            store(T - 3)
            load(T - 1, 0, False)
            store(T - 2)
            store(T - 1)
            sp.wait_ge(stored, 16 * T)

        @block.gpsimd
        def _(pool):
            pool.memset(half[:], -0.5).then_inc(half_made, 1)
            pool.wait_ge(half_made, 1)
            pool.wait_ge(var_made, 1)
            pool.tensor_tensor(rstd[:], var[:], half[:], ALU.pow).then_inc(rstd_made, 1)

        @block.scalar
        def _(act):
            act.wait_ge(ex_in, 1)
            act.activation(ex[:], lg[:], ACT.Exp).then_inc(ex_out, 1)
            act.wait_ge(ex_in, 2)
            act.activation(gate[:], sc[:], ACT.Exp).then_inc(ex_out, 1)

        @block.vector
        def _(v):
            step = Chain(v, v_step)

            def tt(out, a, b, op):
                step(v.tensor_tensor(out, a, b, op))

            def wide(ap, n):
                return ap.unsqueeze(2).broadcast_to([P, T, n])

            hd = keep.h
            tt(lg[:], hd[:, :, HC:R2], hd[:, :, R2:R2 + H2], ALU.add)
            tt(lb[:], hd[:, :, R2:R2 + H2], keep.amax[:].unsqueeze(1).broadcast_to([P, T, H2]), ALU.add)
            step(v.scalar_tensor_tensor(lg[:], lg[:], 0.2, lg[:], ALU.mult, ALU.max))
            step(v.scalar_tensor_tensor(lb[:], lb[:], 0.2, lb[:], ALU.mult, ALU.max))
            v.tensor_tensor(lg[:], lg[:], lb[:], ALU.subtract).then_inc(ex_in, 1)
            v.wait_ge(ex_out, 1)
            tt(own[:].rearrange("p t (h x) -> p t h x", x=X), hd[:, :, 0:HC].rearrange("p t (h x) -> p t h x", x=X),
               ex[:].unsqueeze(3).broadcast_to([P, T, H2, X]), ALU.mult)
            tt(num[:], keep.agg[:, :, 0:HC], own[:], ALU.add)
            tt(den[:], keep.agg[:, :, HC:R2], ex[:], ALU.add)
            step(v.tensor_scalar(den[:], den[:], 1e-16, None, ALU.add))
            step(v.reciprocal(den[:], den[:]))
            tt(num[:].rearrange("p t (h x) -> p t h x", x=X), num[:].rearrange("p t (h x) -> p t h x", x=X),
               den[:].unsqueeze(3).broadcast_to([P, T, H2, X]), ALU.mult)
            v.wait_ge(loaded, 48)
            tt(num[:], num[:], bg[:].unsqueeze(1).broadcast_to([P, T, HC]), ALU.add)
            step(v.tensor_reduce(mean[:], num[:], AX_X, ALU.add))
            step(v.tensor_scalar(mean[:], mean[:], 1.0 / HC, None, ALU.mult))
            tt(num[:], num[:], wide(mean[:], HC), ALU.subtract)
            tt(sq[:], num[:], num[:], ALU.mult)
            step(v.tensor_reduce(var[:], sq[:], AX_X, ALU.add))
            v.tensor_scalar(var[:], var[:], 1.0 / HC, EPS_LN, ALU.mult, ALU.add).then_inc(var_made, 1)
            v.wait_ge(rstd_made, 1)
            tt(num[:], num[:], wide(rstd[:], HC), ALU.mult)
            tt(num[:], num[:], gam[:].unsqueeze(1).broadcast_to([P, T, HC]), ALU.mult)
            tt(num[:], num[:], bet[:].unsqueeze(1).broadcast_to([P, T, HC]), ALU.add)
            step(v.tensor_reduce(sc[:], num[:].rearrange("p t (h x) -> p t x h", x=X), AX_X, ALU.add))
            step(v.tensor_scalar(sc[:], sc[:], 1.0 / H2, None, ALU.mult))
            step(v.memset(rank[:], 0.0))
            for a in range(X):
                for o in range(X):
                    if o != a:
                        tt(beat[:], sc[:, :, o], sc[:, :, a], ALU.is_ge if o < a else ALU.is_gt)
                        tt(rank[:, :, a], rank[:, :, a], beat[:], ALU.add)
            step(v.tensor_reduce(top[:], sc[:], AX_X, ALU.max))
            v.tensor_tensor(sc[:], sc[:], wide(top[:], X), ALU.subtract).then_inc(ex_in, 1)
            step(v.tensor_scalar(rank[:], rank[:], 2.0, None, ALU.is_lt))
            v.wait_ge(ex_out, 2)
            tt(gate[:], gate[:], rank[:], ALU.mult)
            step(v.tensor_reduce(total[:], gate[:], AX_X, ALU.add))
            step(v.reciprocal(total[:], total[:]))
            tt(gate[:], gate[:], wide(total[:], X), ALU.mult)

            def add_experts(t, b, turn):
                wait(v, y_loaded[b], turn * 16)
                xr = keep.x[:, bass.ds(t, 1), :].rearrange("p a c -> p (a c)")
                for x in range(X):
                    ins = v.scalar_tensor_tensor(xr, y[b][:, x, :],
                                                 gate[:, bass.ds(t, 1), x:x + 1].rearrange("p a c -> p (a c)"), xr,
                                                 ALU.mult, ALU.add)
                    if x < X - 1:
                        step(ins)
                ins.then_inc(summed, 1)

            with v.Fori(0, T // 2) as i:
                step.enter(i, 2 * (X - 1))
                for b in range(2):
                    add_experts(i * 2 + b, b, i + 1)
                step.leave(T // 2)
            add_experts(T - 1, 0, T // 2 + 1)


class Keep:

    def __init__(self, nc, ctx):
        def sb(name, shape, dt=F32):
            return ctx.enter_context(nc.sbuf_tensor(name, shape, dt))

        self.x = sb("x_sb", [P, T, C])
        self.xT = sb("xT_sb", [P, CB, NT])
        self.ident = sb("ident", [P, P])
        self.iota = sb("iota", [P, P])
        self.sel8 = sb("sel8", [P, H])
        self.ones = sb("ones", [P, P])
        self.vrow = sb("vrow", [1, NT], BF16)
        self.ee = sb("ee", [P, T * PAIRS * 2 * H])
        self.bound = sb("bound", [P, H])
        self.base = sb("base", [P, G1 + 1], I32)
        self.rel = sb("rel", [P, G1 + 1, K4])
        self.accF = sb("accF", [P, CB, NW])
        self.accD = sb("accD", [P, NW])
        self.h = sb("h", [P, T, HC + 2 * H2])
        self.amax = sb("amax_k", [P, H2])
        self.agg = sb("agg_k", [P, T, R2])


class Scratch:

    def __init__(self, nc):
        self.table = nc.dram_tensor("source_table", [NT, TF], F32).ap()
        self.et = nc.dram_tensor("target_scores", [NW, 3 * H], BF16).ap()
        self.source = nc.dram_tensor("source_table2", [NT, R2], F32).ap()
        self.target = nc.dram_tensor("target_scores2", [NT, H2], F32).ap()
        self.y = nc.dram_tensor("expert_out", [NT, X * C], F32).ap()


def build(nc, io):
    with ExitStack() as ctx:
        keep = Keep(nc, ctx)
        dram = Scratch(nc)
        prepare(nc, io, keep, dram)
        attend(nc, io, keep, dram)
        combine(nc, io, keep, dram)
        experts(nc, io, keep, dram)
        route(nc, io, keep, dram)


def kernel(**inputs):
    import numpy as np
    import concourse.bacc as bacc
    from concourse import mybir as _mybir
    from concourse.bass_utils import run_bass_kernel_spmd

    a = {k: np.asarray(v) for k, v in inputs.items()}

    def pad(v, rows, value=0):
        return np.concatenate([v, np.full((rows - v.shape[0],) + v.shape[1:], value, v.dtype)])

    src = pad(a["src"], (G1 + 1) * GE).reshape(G1 + 1, K4, P).transpose(0, 2, 1)
    dst = pad(a["dst"], (G1 + 1) * GE, -1).reshape(G1 + 1, K4, P).transpose(2, 0, 1)
    pairs = (T + 1) * PAIRS
    edge = pad(a["edge_attr_64"], pairs * 2 * P).reshape(pairs, 2, P, ED).transpose(1, 3, 0, 2).reshape(2 * ED, pairs * P)
    e2 = a["L0_ffn_edge_index"].reshape(2, G2, K4, P)
    arrays = {
        "x": pad(a["x"], NT),
        "src": src, "dst": dst, "edge": edge,
        "W_fc": a["L0_gnn_W_fc"], "W_e": a["L0_gnn_W_e"],
        "attn_h": a["L0_gnn_attn_h"].reshape(1, C), "attn_e": a["L0_gnn_attn_e"].reshape(1, C),
        "attn_t": a["L0_gnn_attn_t"].reshape(1, C), "bias": a["L0_gnn_bias"].reshape(1, C),
        "WqkvT": a["L0_mix_Wqkv"].T, "bqkv": a["L0_mix_bqkv"].reshape(1, 3 * C),
        "WprojT": a["L0_mix_Wproj"].T, "bproj": a["L0_mix_bproj"].reshape(1, C),
        "temp": a["L0_mix_temperature"].reshape(1, H),
        "W_gat": a["L0_ffn_W_gat"], "att_src": a["L0_ffn_att_src"].reshape(1, HC),
        "att_dst": a["L0_ffn_att_dst"].reshape(1, HC), "b_gat": a["L0_ffn_b_gat"].reshape(1, HC),
        "ln_gamma": a["L0_ffn_ln_gamma"].reshape(1, HC), "ln_beta": a["L0_ffn_ln_beta"].reshape(1, HC),
        "W1": a["L0_ffn_W1"], "b1": a["L0_ffn_b1"].reshape(X * HB, P).T,
        "W2": a["L0_ffn_W2"], "b2": a["L0_ffn_b2"].reshape(1, X * C),
        "edges2": e2.transpose(3, 0, 1, 2).reshape(P, 2, G2 * K4),
        "idx2": e2.transpose(1, 3, 0, 2).reshape(G2, P, 2 * K4),
    }
    arrays = {k: np.ascontiguousarray(v) for k, v in arrays.items()}
    nc = bacc.Bacc("TRN2", target_bir_lowering=False, num_devices=1)
    io = {k: nc.dram_tensor(f"in_{k}", v.shape, _mybir.dt.from_np(v.dtype), kind="ExternalInput").ap()
          for k, v in arrays.items()}
    io["out"] = nc.dram_tensor("out", (NT, C), _mybir.dt.float32, kind="ExternalOutput").ap()
    build(nc, io)
    r = run_bass_kernel_spmd(nc, [{f"in_{k}": v for k, v in arrays.items()}], core_ids=[0])
    return r.results[0]["out"][:N]
```
